# Optimizing a Trainium2 kernel written in Bass

```python
import numpy as np
import jax
import jax.numpy as jnp

def _softmax(x, axis=-1):
    return jax.nn.softmax(x, axis=axis)

def _gelu(x):
    return jax.nn.gelu(x, approximate=True)

def _silu(x):
    return jax.nn.silu(x)

def _sigmoid(x):
    return jax.nn.sigmoid(x)

def _layernorm(x, axis=-1, eps=1e-05):
    m = jnp.mean(x, axis=axis, keepdims=True)
    v = jnp.var(x, axis=axis, keepdims=True)
    return (x - m) / jnp.sqrt(v + eps)

def _scatter_add(tgt, idx, src, axis=0):
    return tgt.at[idx].add(src)

def _segment_sum(src, seg, n):
    return jax.ops.segment_sum(src, seg, n)
kernel_name = 'mk_gnn_preln_d2_gnn_r16_468551'

def setup_inputs(seed: int=0):
    np.random.seed(seed)
    _w = jnp.asarray

    def _rec_inputs():
        import jax
        import jax.numpy as jnp
        _gk = jax.random.key(seed)
        x = -0.0003713 + 1 * jax.random.normal(jax.random.fold_in(_gk, 1), (3125, 128), jnp.float32)
        _s = jax.random.randint(jax.random.fold_in(_gk, 2), (25000,), 0, 3125, jnp.int32)
        _d = jax.random.randint(jax.random.fold_in(_gk, 3), (25000,), 0, 3125, jnp.int32)
        _loop = jnp.arange(3125, dtype=jnp.int32)
        src = jnp.concatenate([_s, _d, _loop])
        dst = jnp.concatenate([_d, _s, _loop])
        _o = jnp.argsort(dst, stable=True)
        src = src[_o]
        dst = dst[_o]
        edge_type_8 = jax.random.randint(jax.random.fold_in(_gk, 12), (53125,), 0, 8, jnp.int32)
        return (x, src, dst, edge_type_8)
    x, src, dst, edge_type_8 = _rec_inputs()

    def _L0_gnn_setup():
        import jax, jax.numpy as jnp
        import numpy as np
        NUM_RELATIONS = 8

        def rgcn_conv(x, edge_index, edge_type, W, root, bias):
            src, dst = (edge_index[0], edge_index[1])
            N = x.shape[0]
            out = x @ root + bias
            for r in range(NUM_RELATIONS):
                mask = edge_type == r
                h = x @ W[r]
                msg = jnp.where(mask[:, None], h[src], jnp.zeros((), x.dtype))
                agg = jax.ops.segment_sum(msg, dst, num_segments=N)
                cnt = jax.ops.segment_sum(mask.astype(x.dtype), dst, num_segments=N)
                out = out + agg / jnp.maximum(cnt, 1.0)[:, None]
            return out
        key = jax.random.key(seed)
        ks = jax.random.split(key, 16)
        N, E, Fin, H, R = (6250, 37500, 128, 128, NUM_RELATIONS)
        x = jax.random.normal(ks[0], (N, Fin), dtype=jnp.float32)
        edge_index = jax.random.randint(ks[1], (2, E), 0, N, dtype=jnp.int64)
        edge_type = jax.random.randint(ks[2], (E,), 0, R, dtype=jnp.int64)
        s = 0.05
        return {'x': x, 'edge_index': edge_index, 'edge_type': edge_type, 'W1': jax.random.normal(ks[3], (R, Fin, H), dtype=jnp.float32) * s, 'root1': jax.random.normal(ks[4], (Fin, H), dtype=jnp.float32) * s, 'b1': jnp.zeros((H,), dtype=jnp.float32), 'W2': jax.random.normal(ks[5], (R, H, H), dtype=jnp.float32) * s, 'root2': jax.random.normal(ks[6], (H, H), dtype=jnp.float32) * s, 'b2': jnp.zeros((H,), dtype=jnp.float32), 'W3': jax.random.normal(ks[7], (R, H, H), dtype=jnp.float32) * s, 'root3': jax.random.normal(ks[8], (H, H), dtype=jnp.float32) * s, 'b3': jnp.zeros((H,), dtype=jnp.float32)}
    _L0_gnn_all = _L0_gnn_setup()
    _L0_gnn_in = {k: v for k, v in _L0_gnn_all.items() if k in ('W1', 'root1', 'b1', 'W2', 'root2', 'b2', 'W3', 'root3', 'b3')}
    del _L0_gnn_all

    def _L1_gnn_setup():
        import jax, jax.numpy as jnp
        import numpy as np
        N_NODES = 3125
        N_EDGES = 50000
        D_IN = 128
        D_HID = 128
        BN_EPS = 1e-05
        key = jax.random.key(seed)
        ks = jax.random.split(key, 8)
        x = jax.random.normal(ks[0], (N_NODES, D_IN), dtype=jnp.float32)
        edge_index = jax.random.randint(ks[1], (2, N_EDGES), 0, N_NODES, dtype=jnp.int32)
        W1 = jax.random.normal(ks[2], (D_IN, D_HID), dtype=jnp.float32) * (1.0 / np.sqrt(D_IN))
        b1 = jnp.zeros((D_HID,), dtype=jnp.float32)
        W2 = jax.random.normal(ks[3], (D_HID, D_IN), dtype=jnp.float32) * (1.0 / np.sqrt(D_HID))
        b2 = jnp.zeros((D_IN,), dtype=jnp.float32)
        gamma = jnp.ones((D_IN,), dtype=jnp.float32)
        beta = jnp.zeros((D_IN,), dtype=jnp.float32)
        return {'x': x, 'edge_index': edge_index, 'W1': W1, 'b1': b1, 'W2': W2, 'b2': b2, 'gamma': gamma, 'beta': beta}
    _L1_gnn_all = _L1_gnn_setup()
    _L1_gnn_in = {k: v for k, v in _L1_gnn_all.items() if k in ('W1', 'b1', 'W2', 'b2', 'gamma', 'beta')}
    del _L1_gnn_all
    return {'x': x, 'src': src, 'dst': dst, 'edge_type_8': edge_type_8, 'L0_gnn_W1': _L0_gnn_in['W1'], 'L0_gnn_root1': _L0_gnn_in['root1'], 'L0_gnn_b1': _L0_gnn_in['b1'], 'L0_gnn_W2': _L0_gnn_in['W2'], 'L0_gnn_root2': _L0_gnn_in['root2'], 'L0_gnn_b2': _L0_gnn_in['b2'], 'L0_gnn_W3': _L0_gnn_in['W3'], 'L0_gnn_root3': _L0_gnn_in['root3'], 'L0_gnn_b3': _L0_gnn_in['b3'], 'L1_gnn_W1': _L1_gnn_in['W1'], 'L1_gnn_b1': _L1_gnn_in['b1'], 'L1_gnn_W2': _L1_gnn_in['W2'], 'L1_gnn_b2': _L1_gnn_in['b2'], 'L1_gnn_gamma': _L1_gnn_in['gamma'], 'L1_gnn_beta': _L1_gnn_in['beta']}

def reference(x, src, dst, edge_type_8, L0_gnn_W1, L0_gnn_root1, L0_gnn_b1, L0_gnn_W2, L0_gnn_root2, L0_gnn_b2, L0_gnn_W3, L0_gnn_root3, L0_gnn_b3, L1_gnn_W1, L1_gnn_b1, L1_gnn_W2, L1_gnn_b2, L1_gnn_gamma, L1_gnn_beta):
    import jax
    import jax.numpy as jnp

    def _L0_gnn_ref(x, edge_index, edge_type, W1, root1, b1, W2, root2, b2, W3, root3, b3):
        import jax, jax.numpy as jnp
        import numpy as np
        NUM_RELATIONS = 8

        def rgcn_conv(x, edge_index, edge_type, W, root, bias):
            src, dst = (edge_index[0], edge_index[1])
            N = x.shape[0]
            out = x @ root + bias
            for r in range(NUM_RELATIONS):
                mask = edge_type == r
                h = x @ W[r]
                msg = jnp.where(mask[:, None], h[src], jnp.zeros((), x.dtype))
                agg = jax.ops.segment_sum(msg, dst, num_segments=N)
                cnt = jax.ops.segment_sum(mask.astype(x.dtype), dst, num_segments=N)
                out = out + agg / jnp.maximum(cnt, 1.0)[:, None]
            return out
        h = jax.nn.relu(rgcn_conv(x, edge_index, edge_type, W1, root1, b1))
        h = jax.nn.relu(rgcn_conv(h, edge_index, edge_type, W2, root2, b2))
        h = jax.nn.relu(rgcn_conv(h, edge_index, edge_type, W3, root3, b3))
        return h

    def _L1_gnn_ref(x, edge_index, W1, b1, W2, b2, gamma, beta):
        import jax, jax.numpy as jnp
        import numpy as np
        N_NODES = 3125
        N_EDGES = 50000
        D_IN = 128
        D_HID = 128
        BN_EPS = 1e-05
        n = x.shape[0]
        src, dst = (edge_index[0], edge_index[1])
        aggr = jax.ops.segment_sum(x[src], dst, num_segments=n)
        h = x + aggr
        h = jax.nn.relu(h @ W1 + b1) @ W2 + b2
        mean = jnp.mean(h, axis=0)
        var = jnp.var(h, axis=0)
        h = (h - mean) * jax.lax.rsqrt(var + BN_EPS) * gamma + beta
        return h + x
    edge_index = jnp.stack([src, dst])
    h = jnp.maximum(_layernorm(x, axis=-1), 0.0)
    x = x + _L0_gnn_ref(h, edge_index, edge_type_8, L0_gnn_W1, L0_gnn_root1, L0_gnn_b1, L0_gnn_W2, L0_gnn_root2, L0_gnn_b2, L0_gnn_W3, L0_gnn_root3, L0_gnn_b3)
    h = jnp.maximum(_layernorm(x, axis=-1), 0.0)
    x = x + _L1_gnn_ref(h, edge_index, L1_gnn_W1, L1_gnn_b1, L1_gnn_W2, L1_gnn_b2, L1_gnn_gamma, L1_gnn_beta)
    return x

_drawn_inputs = setup_inputs


def setup_inputs(seed=0):
    import zlib

    import numpy as np

    out = dict(_drawn_inputs(seed))
    spreads = {'L0_gnn_b1': (0.0, 0.1),
     'L0_gnn_b2': (0.0, 0.1),
     'L0_gnn_b3': (0.0, 0.1),
     'L1_gnn_b1': (0.0, 0.8),
     'L1_gnn_b2': (0.0, 0.8),
     'L1_gnn_gamma': (1.0, 0.2),
     'L1_gnn_beta': (0.0, 0.1)}
    factors = {}
    for name, (base, spread) in spreads.items():
        noise = np.random.default_rng([zlib.crc32(name.encode()), seed]).standard_normal(out[name].shape)
        drawn = base * np.exp(spread * noise) if base else spread * noise
        out[name] = jnp.asarray(drawn.astype(out[name].dtype))
    for name, factor in factors.items():
        out[name] = (out[name] * factor).astype(out[name].dtype)
    return out
```

```python
from contextlib import ExitStack

import concourse.bass as bass
from concourse import mybir

ALU = mybir.AluOpType
ACT = mybir.ActivationFunctionType
F32 = mybir.dt.float32
I32 = mybir.dt.int32
ds = bass.ds

P = 128
REL = 8
WIN = 16
LAYERS = 4
GIN = LAYERS - 1
LAST_REL = GIN - 1
LN_EPS = 1e-5
BN_EPS = 1e-5
LAG = 4
FREE = 1
AHEAD = 4
OFFS = 20


def cdiv(a, b):
    return -(-a // b)


def plan(nodes, edges):
    tiles = cdiv(edges, P)
    blocks = cdiv(nodes, P)
    per_block = cdiv(tiles, cdiv(nodes * 1, P)) if nodes % P == 0 else cdiv(edges * P, nodes * P)
    assert (blocks - 1) * per_block < tiles <= blocks * per_block and per_block <= OFFS
    assert blocks % 2 == 1 and blocks >= 5
    return tiles, blocks, per_block


def gnn_kernel(nc, x, src_t, dst_t, type_t, limits, w_rel, root_w, bias_w,
               gin_w1, gin_b1, gin_w2, gin_b2, gamma, beta, out, tables, EDGES):
    N, D = x.shape
    TILES, BLOCKS, TPB = plan(N, EDGES)
    LAST = BLOCKS - 1
    ND_LAST = N - LAST * P
    T_LAST = TILES - LAST * TPB
    KEYS = P * REL
    RING = 2 * P
    COLS = TPB * BLOCKS
    S_USES = lambda i: BLOCKS if i < T_LAST else BLOCKS - 1

    with ExitStack() as ctx:
        def sb(name, shape, dt=F32):
            return ctx.enter_context(nc.sbuf_tensor(name, shape, dt))

        def sem(name):
            return ctx.enter_context(nc.semaphore(name))

        x_rows = sb("x_rows", [P, BLOCKS, D])
        hT = [sb("hT0", [P, BLOCKS * P]), sb("hT1", [P, BLOCKS * P])]
        recip = sb("recip", [P, BLOCKS * KEYS])
        sums = sb("sums", [P, (RING + WIN) * REL])
        counts = sb("counts", [P, (RING + WIN) * REL])
        rows = sb("rows", [P, TPB, D])
        sel = sb("sel", [P, TPB, P])
        scaled = sb("scaled", [P, REL, P])
        w_all = sb("w_all", [P, GIN, REL + 1, D])
        w_gin = sb("w_gin", [P, 2, D])
        vecs = sb("vecs", [P, 8])
        src_i = sb("src_i", [P, COLS], I32)
        idx = sb("idx", [P, 2, TPB], I32)
        relk = sb("relk", [P, COLS])
        reld = sb("reld", [P, COLS])
        key = sb("key", [P, COLS])
        dst_f = sb("dst_f", [P, COLS])
        gen_key = sb("gen_key", [P, COLS])
        offk = sb("offk", [P, BLOCKS, OFFS], I32)
        offd = sb("offd", [P, BLOCKS, OFFS], I32)
        ident = sb("ident", [P, P])
        iota = sb("iota", [P, P])
        ones = sb("ones", [P, P])
        hid = sb("hid", [P, P])
        row_out = sb("row_out", [P, 2, D])
        x1, xn = counts[:, 0:D], counts[:, D:2 * D]
        small = sb("small", [P, 8])
        stat = sb("stat", [P, 6])
        mv = sb("mv", [P, 2])
        bn = recip[:, 0:6 * BLOCKS].rearrange("p (b s) -> p b s", s=6)
        sum_i = sums[:, 0:3 * COLS].bitcast(I32)
        dst_i, type_i, base_i = (sum_i[:, n * COLS:(n + 1) * COLS] for n in range(3))
        cnt_v = counts[:, 0:4 * COLS]
        base_f, type_f, in_win, broke = (cnt_v[:, n * COLS:(n + 1) * COLS] for n in range(4))
        lim = recip[:, 0:2 * COLS].rearrange("p (a t) -> p a t", a=2)
        ln_stat = recip[:, 1024:1024 + 6 * BLOCKS].rearrange("p (b s) -> p b s", s=6)
        ln_mv = recip[:, 2048:2048 + 2 * BLOCKS].rearrange("p (b s) -> p b s", s=2)
        ln_sd = recip[:, 2304:2304 + BLOCKS]
        ln_rs = recip[:, 2432:2432 + BLOCKS]
        h0 = recip[:, 4096:4096 + BLOCKS * D].rearrange("p (b f) -> p b f", f=D)
        xn0 = recip[:, 8192:8192 + BLOCKS * D].rearrange("p (b f) -> p b f", f=D)
        flag = sb("flag", [P, 2], I32)
        iota_i = row_out[:, 0, :].bitcast(I32)

        def bank(name):
            return ctx.enter_context(nc.psum_tensor(name, [P, 512], F32))

        ps_sum = [bank("ps_sum0"), bank("ps_sum1")]
        ps_cnt = [bank("ps_cnt0"), bank("ps_cnt1")]
        ps_fin = bank("ps_fin")
        ps_tr = bank("ps_tr")
        ps_tr2 = bank("ps_tr2")
        ps_misc = bank("ps_misc")

        s_x = sem("s_x")
        s_edges = sem("s_edges")
        s_w = sem("s_w")
        s_pool_const = sem("s_pool_const")
        s_const = sem("s_const")
        s_prep = sem("s_prep")
        s_lnsd = sem("s_lnsd")
        s_xn0 = sem("s_xn0")
        s_h0 = sem("s_h0")
        s_h0tr = sem("s_h0tr")
        s_asked = sem("s_asked")
        s_stats_seen = sem("s_stats_seen")
        s_hid0 = sem("s_hid0")
        s_yout0 = sem("s_yout0")
        s_tab0 = sem("s_tab0")
        s_metric = sem("s_metric")
        s_total = sem("s_total")
        s_flag = sem("s_flag")
        s_ready = sem("s_ready")
        s_idx = sem("s_idx")
        s_g = [sem(f"s_g{i}") for i in range(TPB)]
        s_sel = sem("s_sel")
        s_mm = sem("s_mm")
        s_add = sem("s_add")
        s_fold = sem("s_fold")
        s_cmax = sem("s_cmax")
        s_recip = sem("s_recip")
        s_scaled = sem("s_scaled")
        s_zero = sem("s_zero")
        s_fin = sem("s_fin")
        s_hs = sem("s_hs")
        s_hid = sem("s_hid")
        s_tr = sem("s_tr")
        s_row = sem("s_row")
        s_tab = [sem("s_tab_even"), sem("s_tab_odd")]
        s_x1 = sem("s_x1")
        s_st = sem("s_st")
        s_mv = sem("s_mv")
        s_sd = sem("s_sd")
        s_rs = sem("s_rs")
        s_xn = sem("s_xn")
        s_tr2 = sem("s_tr2")
        s_xh = sem("s_xh")
        s_bn = sem("s_bn")
        s_gen = sem("s_gen")
        s_fin_dve = sem("s_fin_dve")
        s_bnsd = sem("s_bnsd")
        s_y = sem("s_y")
        s_ytr = sem("s_ytr")
        s_yout = sem("s_yout")
        s_store = [sem("s_store0"), sem("s_store1")]

        n_pool_const = 2
        FULL = LAST * P

        def width(L):
            return REL if L < GIN else 1

        def close_scale(dve, L, j, nd, col, fold, adds, folds, **_):
            kw, G = width(L), BLOCKS * L + j
            blk = slice(col * kw, (col + nd) * kw)
            spill = slice(RING * kw, (RING + WIN) * kw)
            dve.wait_ge(s_add, adds)
            if fold:
                front = slice(0, WIN * kw)
                fold_of_sums = nc.vector.tensor_tensor(sums[:, front], sums[:, front], sums[:, spill], ALU.add)
                if L == 0:
                    nc.vector.tensor_tensor(counts[:, front], counts[:, front], counts[:, spill],
                                            ALU.add).then_inc(s_fold, 1)
                else:
                    fold_of_sums.then_inc(s_fold, 1)
                dve.wait_ge(s_fold, folds)
            if L == 0:
                nc.vector.tensor_scalar(counts[:, blk], counts[:, blk], 1.0, None, ALU.max).then_inc(s_cmax, 1)
                dve.wait_ge(s_cmax, G + 1)
                nc.vector.reciprocal(recip[:, ds(j * KEYS, nd * REL)], counts[:, blk]).then_inc(s_recip, 1)
                dve.wait_ge(s_recip, G + 1)
            dve.wait_ge(s_fin, G + FREE)
            if L < GIN:
                nc.vector.tensor_tensor(
                    scaled[:, :, 0:nd], sums[:, blk].rearrange("p (d r) -> p r d", r=REL),
                    recip[:, ds(j * KEYS, nd * REL)].rearrange("p (d r) -> p r d", r=REL),
                    ALU.mult).then_inc(s_scaled, 1)
            else:
                nc.vector.tensor_tensor(scaled[:, 0, 0:nd], sums[:, blk], hT[L % 2][:, ds(j * P, nd)],
                                        ALU.add).then_inc(s_scaled, 1)
            dve.wait_ge(s_scaled, G + 1)
            if L == 0:
                nc.vector.memset(counts[:, blk], 0.0)
                if fold:
                    nc.vector.memset(counts[:, spill], 0.0)
            if fold:
                nc.vector.memset(sums[:, spill], 0.0)
            nc.vector.memset(sums[:, blk], 0.0).then_inc(s_zero, 1)
            dve.wait_ge(s_zero, G + 1)

        def close_product(pe, L, j, nd, **_):
            G = BLOCKS * L + j
            pe.wait_ge(s_scaled, G + 1)
            pe.wait_ge(s_hid, G + FREE)
            if L < GIN:
                for r in range(REL):
                    nc.tensor.matmul(ps_fin[:, 0:nd], w_all[:, L, r, :], scaled[:, r, 0:nd],
                                     start=(r == 0), stop=False)
                nc.tensor.matmul(ps_fin[:, 0:nd], w_all[:, L, REL, :], hT[L % 2][:, ds(j * P, nd)],
                                 start=False, stop=True).then_inc(s_fin, 1)
            else:
                nc.tensor.matmul(ps_fin[:, 0:nd], w_gin[:, 0, :], scaled[:, 0, 0:nd],
                                 start=True, stop=True).then_inc(s_fin, 1)

        def close_turn(pe, L, j, nd, **_):
            G = BLOCKS * L + j
            pe.wait_ge(s_hs, G + 1)
            if L < LAST_REL:
                pe.wait_ge(s_row, G + FREE)
            elif L == LAST_REL:
                pe.wait_ge(s_x1, j + FREE)
            if L < GIN:
                nc.tensor.transpose(ps_tr[0:nd, 0:D], hid[:, 0:nd], ident[:]).then_inc(s_tr, 1)
            else:
                nc.tensor.matmul(ps_tr[:, 0:nd], w_gin[:, 1, :], hid[:, 0:nd],
                                 start=True, stop=True).then_inc(s_tr, 1)

        def close_turn_back(pe, L, j, nd, p, **_):
            G = BLOCKS * L + j
            if L == LAST_REL:
                pe.wait_ge(s_row, G + 1 + FREE)
                pe.wait_ge(s_hid, G + FREE)
                nc.tensor.transpose(ps_tr2[:, 0:nd], row_out[0:nd, p, :], ident[0:nd, 0:nd]).then_inc(s_tr2, 1)

        def close_scalar(act, L, j, nd, p, before, **_):
            G = BLOCKS * L + j
            nxt = hT[(L + 1) % 2]
            act.wait_ge(s_fin, G + 1 + FREE)
            act.wait_ge(s_tr, G + FREE)
            if L == GIN:
                nc.scalar.activation(hid[:, 0:nd], ps_fin[:, 0:nd], ACT.Relu, bias=vecs[:, 3:4]).then_inc(s_hs, 1)
                act.wait_ge(s_tr, G + 1 + FREE)
                nc.scalar.activation(nxt[:, ds(j * P, nd)], ps_tr[:, 0:nd], ACT.Identity,
                                     bias=vecs[:, 4:5]).then_inc(s_hid, 1)
                return
            nc.scalar.activation(hid[:, 0:nd], ps_fin[:, 0:nd], ACT.Relu, bias=vecs[:, L:L + 1]).then_inc(s_hs, 1)
            if L < LAST_REL:
                nc.scalar.activation(nxt[:, ds(j * P, nd)], ps_fin[:, 0:nd], ACT.Relu,
                                     bias=vecs[:, L:L + 1]).then_inc(s_hid, 1)
                act.wait_ge(s_tr, G + 1 + FREE)
                act.wait_ge(s_tab[p], before * 16 + 16)
                nc.scalar.copy(row_out[0:nd, p, :], ps_tr[0:nd, 0:D]).then_inc(s_row, 1)
            else:
                act.wait_ge(s_mv, j + 1)
                nc.scalar.activation(small[0:nd, 0:1], mv[0:nd, 1:2], ACT.Sqrt, bias=vecs[0:nd, 7:8]).then_inc(s_sd, 1)
                act.wait_ge(s_xn, j + 1)
                act.wait_ge(s_tab[p], before * 16 + 16)
                act.wait_ge(s_xh, j + FREE)
                nc.scalar.activation(row_out[0:nd, p, :], xn[0:nd, :], ACT.Relu).then_inc(s_row, 1)
                act.wait_ge(s_tr2, j + 1)
                nc.scalar.copy(nxt[:, ds(j * P, nd)], ps_tr2[:, 0:nd]).then_inc(s_hid, 1)

        def close_residual(dve, L, j, nd, **_):
            if L == LAST_REL:
                dve.wait_ge(s_tr, BLOCKS * L + j + 1 + FREE)
                dve.wait_ge(s_xh, j + FREE)
                nc.vector.tensor_tensor(x1[0:nd, :], ps_tr[0:nd, 0:D], x_rows[0:nd, j, :] if isinstance(j, int)
                                        else x_rows[0:nd, ds(j, 1), :].rearrange("p a f -> p (a f)"),
                                        ALU.add).then_inc(s_x1, 1)
                dve.wait_ge(s_x1, j + 1 + FREE)
                nc.vector.bn_stats(stat[0:nd, :], x1[0:nd, :]).then_inc(s_st, 1)
                dve.wait_ge(s_st, j + 1)
                dve.sem_inc(s_stats_seen, 1)
                nc.vector.bn_aggr(mv[0:nd, :], stat[0:nd, :]).then_inc(s_mv, 1)
            if L == GIN:
                dve.wait_ge(s_hid, BLOCKS * L + j + 1 + FREE)
                nc.vector.bn_stats(bn[:, j, :] if isinstance(j, int)
                                   else bn[:, ds(j, 1), :].rearrange("p a s -> p (a s)"),
                                   hT[(L + 1) % 2][:, ds(j * P, nd)]).then_inc(s_bn, 1)

        def close_norm(dve, L, j, nd, **_):
            if L == LAST_REL:
                dve.wait_ge(s_sd, j + 1)
                nc.vector.reciprocal(small[0:nd, 1:2], small[0:nd, 0:1]).then_inc(s_rs, 1)
                dve.wait_ge(s_rs, j + 1)
                dve.wait_ge(s_row, BLOCKS * L + j + FREE)
                nc.vector.tensor_scalar(xn[0:nd, :], x1[0:nd, :], mv[0:nd, 0:1], small[0:nd, 1:2],
                                        ALU.subtract, ALU.mult).then_inc(s_xn, 1)

        def close_keep(dve, L, j, nd, p, **_):
            if L == LAST_REL:
                dve.wait_ge(s_row, BLOCKS * L + j + 1 + FREE)
                dve.wait_ge(s_xn, j + 1)
                nc.vector.tensor_tensor(
                    x_rows[0:nd, j, :] if isinstance(j, int)
                    else x_rows[0:nd, ds(j, 1), :].rearrange("p a f -> p (a f)"),
                    x1[0:nd, :], row_out[0:nd, p, :], ALU.add).then_inc(s_xh, 1)

        def close_store(sp, L, j, nd, p, **_):
            if L < GIN:
                sp.wait_ge(s_row, BLOCKS * L + j + 1 + FREE)
                sp.dma_start(tables[L + 1][ds(j * P, nd), :], row_out[0:nd, p, :]).then_inc(s_tab[p], 16)

        def all_stages(eng, stages, **block):
            for _, stage in stages:
                stage(eng, **block)

        def walk(eng, body):
            body(0, 0, 0, TPB)
            with eng.Fori(0, (BLOCKS - 3) // 2) as k:
                body(2 * k + 1, 1, k, TPB)
                body(2 * k + 2, 0, k + 1, TPB)
            body(LAST - 1, 1, (LAST - 1) // 2, TPB)
            body(LAST, 0, LAST // 2, T_LAST)

        EVEN, ODD = (BLOCKS + 1) // 2, BLOCKS // 2

        def fast_block(L, j, odd, half, adds, nd=P):
            return dict(L=L, j=j, nd=nd, col=P * odd, fold=not odd, adds=adds, p=odd,
                        folds=L * EVEN + half + 1, before=L * (ODD if odd else EVEN) + half)

        def fast_walk(eng, L, stages, tile_work, start=None):
            base = TILES * L

            def body(j, odd, half, tiles):
                if start is not None:
                    start(j, odd, half, tiles)
                closes = not (isinstance(j, int) and j == 0)
                for i in range(max(tiles, 1 + max([at for at, _ in stages], default=0))):
                    for at, stage in stages:
                        if at == i and closes:
                            done = min(i, tiles)
                            stage(eng, **fast_block(L, j - 1, 1 - odd, half - 1 if not odd else half,
                                                    base + j * TPB + done + 2))
                    if i < tiles and tile_work is not None:
                        tile_work(j, odd, i, base + j * TPB + i, tiles)

            walk(eng, body)
            all_stages(eng, stages, **fast_block(L, LAST, 0, LAST // 2, base + TILES + 2, ND_LAST))

        def general_steps(L):
            return REL if L < GIN else 1

        def general_base(L):
            return sum(general_steps(l) * TILES * BLOCKS for l in range(L))

        def general_walk(eng, L, stages, tile_work, start=None, end=None):
            steps = general_steps(L)

            def body(j, nd):
                if start is not None:
                    start(j)
                step0 = general_base(L) + j * (TILES * steps)
                if tile_work is not None:
                    with eng.Fori(0, TILES) as t:
                        tile_work(t, BLOCKS * TILES * L + j * TILES + t, step0 + t * steps)
                all_stages(eng, stages, L=L, j=j, nd=nd, col=0, fold=False, folds=0, p=0,
                           adds=step0 + TILES * steps + 2, before=BLOCKS * L + j)
                if end is not None:
                    end(j)

            with eng.Fori(0, LAST) as j:
                body(j, P)
            body(LAST, ND_LAST)

        def wait_table(eng, L, fast):
            if L == 0:
                eng.wait_ge(s_tab0, 32)
            elif fast:
                eng.wait_ge(s_tab[0], 16 * (L * EVEN + FREE))
                eng.wait_ge(s_tab[1], 16 * (L * ODD + FREE))
            else:
                eng.wait_ge(s_tab[0], 16 * (L * BLOCKS + FREE))

        V_STAGES = [(LAG, close_scale), (LAG + 5, close_residual), (LAG + 7, close_norm), (LAG + 9, close_keep)]
        T_STAGES = [(LAG + 2, close_product), (LAG + 4, close_turn), (LAG + 8, close_turn_back)]
        A_STAGES = [(0, close_scalar)]
        S_STAGES = [(0, close_store)]
        block = ctx.enter_context(nc.Block())

        @block.sync
        def _(sp):
            for buffer_free in s_tab:
                sp.sem_inc(buffer_free, 16 * FREE)
            sp.dma_start(x_rows[:, 0:LAST, :], x[0:FULL, :].rearrange("(b p) f -> p b f", p=P)).then_inc(s_x, 16)
            sp.dma_start(x_rows[0:ND_LAST, LAST, :], x[FULL:N, :]).then_inc(s_x, 16)
            sp.dma_start(dst_i, dst_t).then_inc(s_edges, 16)
            sp.dma_start(type_i, type_t).then_inc(s_edges, 16)
            sp.dma_start(base_i, dst_t[0:1, :].broadcast_to([P, COLS])).then_inc(s_edges, 16)
            sp.dma_start(src_i[:], src_t).then_inc(s_edges, 16)
            for a in range(2):
                sp.dma_start(lim[:, a, :], limits[a:a + 1, :].broadcast_to([P, COLS])).then_inc(s_edges, 16)
            for L in range(GIN):
                sp.dma_start(w_all[:, L, 0:REL, :], w_rel[L].rearrange("r f o -> f r o")).then_inc(s_w, 16)
                sp.dma_start(w_all[:, L, REL, :], root_w[L]).then_inc(s_w, 16)
                sp.dma_start(vecs[:, L:L + 1], bias_w[L].rearrange("(p o) -> p o", o=1)).then_inc(s_w, 16)
            sp.dma_start(w_gin[:, 0, :], gin_w1).then_inc(s_w, 16)
            sp.dma_start(w_gin[:, 1, :], gin_w2).then_inc(s_w, 16)
            for n, v in enumerate((gin_b1, gin_b2, gamma, beta)):
                sp.dma_start(vecs[:, 3 + n:4 + n], v.rearrange("(p o) -> p o", o=1)).then_inc(s_w, 16)
            sp.wait_ge(s_h0, 2)
            sp.dma_start(tables[0][0:FULL, :].rearrange("(b p) f -> p b f", p=P), h0[:, 0:LAST, :]).then_inc(s_tab0, 16)
            sp.dma_start(tables[0][FULL:N, :], h0[0:ND_LAST, LAST, :]).then_inc(s_tab0, 16)
            sp.wait_ge(s_flag, 1)
            fast = sp.value_load(flag[0:1, 0:1], min_val=0, max_val=1)
            with sp.If(fast != 0):
                for L in range(GIN):
                    fast_walk(sp, L, S_STAGES, None)
            with sp.Else():
                for L in range(GIN):
                    general_walk(sp, L, S_STAGES, None)
            for q in range(cdiv(BLOCKS, 4)):
                sp.wait_ge(s_yout, q + 1)
                nb = min(4, BLOCKS - 4 * q)
                stage = sel[:, 4 * (q % 2):4 * (q % 2) + nb, :]
                if nb == 4:
                    sp.dma_start(out[512 * q:512 * (q + 1), :].rearrange("(b p) f -> p b f", p=P),
                                 stage).then_inc(s_store[q % 2], 16)
                else:
                    sp.dma_start(out[FULL:N, :], stage[0:ND_LAST, 0, :]).then_inc(s_store[q % 2], 16)
            NQ = cdiv(BLOCKS, 4)
            sp.wait_ge(s_store[0], 16 * cdiv(NQ, 2))
            sp.wait_ge(s_store[1], 16 * (NQ // 2))

        @block.gpsimd
        def _(pool):
            nc.gpsimd.iota(iota_i, pattern=[[1, P]], base=0, channel_multiplier=0).then_inc(s_pool_const, 1)
            pool.wait_ge(s_const, 2)
            nc.gpsimd.affine_select(out=ident[:], in_=ident[:], compare_op=ALU.not_equal, fill=1.0, base=0,
                                    pattern=[[-1, P]], channel_multiplier=1).then_inc(s_pool_const, 1)
            pool.wait_ge(s_flag, 1)
            fast = pool.value_load(flag[0:1, 0:1], min_val=0, max_val=1)

            def gather(L, slot, column, inc):
                pool.sem_inc(s_asked, 1)
                pool.indirect_dma_start(rows[:, slot, :], None, tables[L],
                                        bass.IndirectOffsetOnAxis(ap=column, axis=0)).then_inc(inc, 16)

            with pool.If(fast != 0):
                for L in range(LAYERS):
                    def index_block(j, odd, half, tiles, L=L):
                        pool.wait_ge(s_idx, BLOCKS * L + j + 1)

                    def tile(j, odd, i, T, tiles, L=L):
                        pool.wait_ge(s_mm, T + 1)
                        gather(L, i, idx[:, odd, i:i + 1], s_g[i])

                    wait_table(pool, L, True)
                    fast_walk(pool, L, [], tile, index_block)
            with pool.Else():
                for L in range(LAYERS):
                    def tile(t, T, step, L=L):
                        pool.wait_ge(s_idx, T + 1)
                        pool.wait_ge(s_mm, step + TPB)
                        gather(L, 0, idx[:, 0, 0:1], s_g[0])

                    wait_table(pool, L, False)
                    general_walk(pool, L, [], tile)

        @block.scalar
        def _(act):
            for buffer_free in (s_hid, s_row):
                act.sem_inc(buffer_free, FREE)
            act.wait_ge(s_prep, 3)
            nc.scalar.activation(ln_sd, ln_mv[:, :, 1], ACT.Sqrt, bias=vecs[:, 7:8]).then_inc(s_lnsd, 1)
            act.wait_ge(s_xn0, 1)
            nc.scalar.activation(h0[:, 0:LAST, :], xn0[:, 0:LAST, :], ACT.Relu).then_inc(s_h0, 1)
            nc.scalar.activation(h0[0:ND_LAST, LAST, :], xn0[0:ND_LAST, LAST, :], ACT.Relu).then_inc(s_h0, 1)
            act.wait_ge(s_edges, 96)
            act.wait_ge(s_flag, 1)
            fast = act.value_load(flag[0:1, 0:1], min_val=0, max_val=1)

            def copy_h0():
                for q in range(cdiv(BLOCKS, 4)):
                    act.wait_ge(s_h0tr, q + 1)
                    n = min(4 * P, N - 4 * P * q)
                    nc.scalar.copy(hT[0][:, 4 * P * q:4 * P * q + n],
                                   (ps_tr, ps_tr2)[q % 2][:, 0:n]).then_inc(s_hid0, 1)

            with act.If(fast != 0):
                for L in range(LAYERS):
                    if L:
                        act.wait_ge(s_mm, TPB + TILES * L)
                    nc.scalar.copy(idx[:, 0, :], src_i[:, 0:TPB]).then_inc(s_idx, 1)
                    if L == 0:
                        copy_h0()

                    def next_index(j, odd, half, tiles, L=L):
                        if isinstance(j, int) and j == LAST:
                            return
                        act.wait_ge(s_mm, TILES * L + j * TPB + TPB)
                        nc.scalar.copy(idx[:, 1 - odd, :], src_i[:, ds((j + 1) * TPB, TPB)]).then_inc(s_idx, 1)

                    fast_walk(act, L, A_STAGES, None, next_index)
            with act.Else():
                copy_h0()
                for L in range(LAYERS):
                    def tile(t, T, step, L=L):
                        act.wait_ge(s_mm, step + TPB)
                        nc.scalar.copy(idx[:, 0, 0:1], src_i[:, ds(t, 1)]).then_inc(s_idx, 1)

                    general_walk(act, L, A_STAGES, tile)
            act.wait_ge(s_fin_dve, 1)
            nc.scalar.activation(small[:, 3:4], small[:, 2:3], ACT.Sqrt, bias=vecs[:, 7:8]).then_inc(s_bnsd, 1)
            act.wait_ge(s_fin_dve, 4)
            flat = scaled[:].rearrange("p r d -> p (r d)")
            for q in range(cdiv(BLOCKS, 4)):
                n = min(4 * P, N - 4 * P * q)
                if q >= 2:
                    act.wait_ge(s_ytr, q - 1)
                nc.scalar.activation(flat[:, 512 * (q % 2):512 * (q % 2) + n], hT[0][:, 4 * P * q:4 * P * q + n],
                                     ACT.Identity, bias=small[:, 6:7], scale=small[:, 5:6]).then_inc(s_y, 1)

        @block.vector
        def _(dve):
            nc.vector.memset(ones[:], 1.0).then_inc(s_const, 1)
            nc.vector.memset(ident[:], 0.0).then_inc(s_const, 1)
            nc.vector.memset(vecs[:, 7:8], LN_EPS).then_inc(s_const, 1)
            nc.vector.memset(ln_mv[:], 1.0).then_inc(s_prep, 1)
            dve.wait_ge(s_prep, 1)
            dve.wait_ge(s_x, 32)
            for b in range(BLOCKS):
                n = P if b < LAST else ND_LAST
                last = nc.vector.bn_stats(ln_stat[0:n, b, :], x_rows[0:n, b, :])
            last.then_inc(s_prep, 1)
            dve.wait_ge(s_prep, 2)
            for b in range(BLOCKS):
                n = P if b < LAST else ND_LAST
                last = nc.vector.bn_aggr(ln_mv[0:n, b, :], ln_stat[0:n, b, :])
            last.then_inc(s_prep, 1)
            dve.wait_ge(s_lnsd, 1)
            nc.vector.reciprocal(ln_rs, ln_sd).then_inc(s_prep, 1)
            dve.wait_ge(s_prep, 4)
            for b in range(BLOCKS):
                n = P if b < LAST else ND_LAST
                last = nc.vector.tensor_scalar(xn0[0:n, b, :], x_rows[0:n, b, :], ln_mv[0:n, b, 0:1],
                                               ln_rs[0:n, b:b + 1], ALU.subtract, ALU.mult)
            last.then_inc(s_xn0, 1)
            dve.wait_ge(s_edges, 96)
            nc.vector.tensor_copy(dst_f[:], dst_i)
            nc.vector.tensor_copy(type_f, type_i)
            nc.vector.tensor_copy(base_f, base_i)
            base_blocks = base_i.rearrange("p (b t) -> p b t", t=TPB)
            nc.vector.memset(offk[:], 0)
            nc.vector.memset(offd[:], 0).then_inc(s_prep, 1)
            dve.wait_ge(s_prep, 5)
            nc.vector.tensor_scalar(offd[:, :, 0:TPB], base_blocks, RING - 1, None, ALU.bitwise_and)
            nc.vector.tensor_scalar(offk[:, :, 0:TPB], base_blocks, RING - 1, 3, ALU.bitwise_and,
                                    ALU.logical_shift_left)
            nc.vector.scalar_tensor_tensor(key[:], dst_f[:], float(REL), type_f, ALU.mult, ALU.add).then_inc(s_prep, 1)
            dve.wait_ge(s_prep, 6)
            nc.vector.scalar_tensor_tensor(relk[:], base_f, -float(REL), key[:], ALU.mult, ALU.add)
            nc.vector.scalar_tensor_tensor(reld[:], base_f, -1.0, dst_f[:], ALU.mult, ALU.add)
            nc.vector.tensor_tensor(type_f[:, 0:TILES], base_f[:, 0:TILES], lim[:, 0, 0:TILES], ALU.is_lt)
            nc.vector.tensor_tensor(broke[:, 0:TILES], base_f[:, 0:TILES], lim[:, 1, 0:TILES],
                                    ALU.is_gt).then_inc(s_prep, 1)
            dve.wait_ge(s_prep, 7)
            nc.vector.tensor_scalar(in_win[:, 0:TILES], relk[:, 0:TILES], 0.0, None, ALU.is_ge)
            nc.vector.tensor_tensor(broke[:, 0:TILES], broke[:, 0:TILES], type_f[:, 0:TILES],
                                    ALU.add).then_inc(s_prep, 1)
            dve.wait_ge(s_prep, 8)
            nc.vector.scalar_tensor_tensor(in_win[:, 0:TILES], relk[:, 0:TILES], float(WIN * REL), in_win[:, 0:TILES],
                                           ALU.is_lt, ALU.mult)
            nc.vector.reduce_sum(small[:, 1:2], broke[:, 0:TILES], mybir.AxisListType.X).then_inc(s_prep, 1)
            dve.wait_ge(s_prep, 9)
            nc.vector.reduce_sum(small[:, 0:1], in_win[:, 0:TILES], mybir.AxisListType.X).then_inc(s_prep, 1)
            dve.wait_ge(s_prep, 10)
            nc.vector.scalar_tensor_tensor(small[:, 2:3], small[:, 1:2], -float(2 * EDGES), small[:, 0:1],
                                           ALU.mult, ALU.add).then_inc(s_metric, 1)
            dve.wait_ge(s_total, 1)
            nc.vector.tensor_scalar(flag[:, 0:1], ps_misc[:, 0:1], float(EDGES), None, ALU.is_equal).then_inc(s_flag, 1)
            dve.wait_ge(s_pool_const, 1)
            nc.vector.tensor_copy(iota[:], iota_i)
            nc.vector.memset(sums[:], 0.0)
            nc.vector.memset(counts[:], 0.0).then_inc(s_ready, 1)
            dve.wait_ge(s_ready, 1)
            dve.sem_inc(s_add, 2)
            for buffer_free in (s_x1, s_xh):
                dve.sem_inc(buffer_free, FREE)
            dve.wait_ge(s_flag, 1)
            dve.wait_ge(s_tab0, 32)
            dve.wait_ge(s_h0tr, cdiv(BLOCKS, 4))
            fast = dve.value_load(flag[0:1, 0:1], min_val=0, max_val=1)
            regs = [dve.alloc_register(f"window_{i}") for i in range(OFFS)]

            def add_tile(L, into, n, psum, T):
                if L == 0:
                    nc.vector.tensor_tensor(sums[:, into], sums[:, into], ps_sum[psum][:, 0:n], ALU.add)
                    nc.vector.tensor_tensor(counts[:, into], counts[:, into], ps_cnt[psum][:, 0:n],
                                            ALU.add).then_inc(s_add, 1)
                else:
                    nc.vector.tensor_tensor(sums[:, into], sums[:, into], ps_sum[psum][:, 0:n],
                                            ALU.add).then_inc(s_add, 1)

            with dve.If(fast != 0):
                for L in range(LAYERS):
                    n = WIN * width(L)
                    rel, off = (relk, offk) if L < GIN else (reld, offd)

                    def select(slot, t, n=n, rel=rel):
                        nc.vector.tensor_scalar(sel[:, slot, 0:n], iota[:, 0:n], rel[:, ds(t, 1)], None,
                                                ALU.is_equal).then_inc(s_sel, 1)

                    def windows(j, odd, half, tiles, off=off):
                        dve.load(regs, off[0:1, j, :] if isinstance(j, int)
                                 else off[0:1, ds(j, 1), :].rearrange("p a t -> p (a t)"))

                    def tile(j, odd, i, T, tiles, L=L, n=n, select=select):
                        if not (isinstance(j, int) and j == LAST and i + AHEAD >= tiles):
                            select((i + AHEAD) % TPB, j * TPB + i + AHEAD)
                        at = dve.snap(regs[i], min_val=0, max_val=(RING - 1) * width(L))
                        dve.wait_ge(s_mm, T + TPB + 1)
                        dve.wait_ge(s_add, T + 2)
                        add_tile(L, ds(at, n), n, (i + odd) % 2, T)

                    if L:
                        dve.wait_ge(s_mm, TPB + TILES * L)
                    for t in range(AHEAD):
                        select(t, t)
                    fast_walk(dve, L, V_STAGES, tile, windows)
            with dve.Else():
                for L in range(LAYERS):
                    n = P

                    def start(j, L=L):
                        if isinstance(j, int):
                            return

                    def tile(t, T, step, L=L, n=n):
                        for c in range(general_steps(L)):
                            dve.wait_ge(s_mm, step + c + TPB)
                            nc.vector.tensor_scalar(sel[:, 0, :], iota[:], float(P * c), gen_key[:, ds(t, 1)],
                                                    ALU.add, ALU.is_equal).then_inc(s_sel, 1)
                            dve.wait_ge(s_mm, step + c + TPB + 1)
                            dve.wait_ge(s_add, step + c + 2)
                            add_tile(L, slice(P * c, P * c + n), n, 0, T)

                    def next_block(j, L=L):
                        nc.vector.tensor_scalar(gen_key[:], gen_key[:], float(P * width(L)), None,
                                                ALU.subtract).then_inc(s_gen, 1)
                        dve.wait_ge(s_gen, (BLOCKS + 1) * L + j + 2)

                    nc.vector.tensor_copy(gen_key[:], key[:] if L < GIN else dst_f[:]).then_inc(s_gen, 1)
                    dve.wait_ge(s_gen, (BLOCKS + 1) * L + 1)
                    general_walk(dve, L, V_STAGES, tile, None, next_block)
            dve.wait_ge(s_bn, BLOCKS)
            nc.vector.bn_aggr(small[:, 1:3], bn[:].rearrange("p b s -> p (b s)")).then_inc(s_fin_dve, 1)
            dve.wait_ge(s_bnsd, 1)
            nc.vector.reciprocal(small[:, 4:5], small[:, 3:4]).then_inc(s_fin_dve, 1)
            dve.wait_ge(s_fin_dve, 2)
            nc.vector.tensor_tensor(small[:, 5:6], small[:, 4:5], vecs[:, 5:6], ALU.mult).then_inc(s_fin_dve, 1)
            dve.wait_ge(s_fin_dve, 3)
            nc.vector.tensor_tensor(small[:, 7:8], small[:, 1:2], small[:, 5:6], ALU.mult).then_inc(s_yout0, 1)
            dve.wait_ge(s_yout0, 1)
            nc.vector.tensor_tensor(small[:, 6:7], vecs[:, 6:7], small[:, 7:8], ALU.subtract).then_inc(s_fin_dve, 1)
            for q in range(cdiv(BLOCKS, 4)):
                nb = min(4, BLOCKS - 4 * q)
                n = P if nb == 4 else ND_LAST
                dve.wait_ge(s_ytr, q + 1)
                if q >= 2:
                    dve.wait_ge(s_store[q % 2], 16 * (q // 2))
                nc.vector.tensor_tensor(sel[0:n, 4 * (q % 2):4 * (q % 2) + nb, :].rearrange("p b f -> p (b f)"),
                                        ps_sum[q % 2][0:n, 0:nb * D],
                                        x_rows[0:n, 4 * q:4 * q + nb, :].rearrange("p b f -> p (b f)"),
                                        ALU.add).then_inc(s_yout, 1)

        @block.tensor
        def _(pe):
            pe.wait_ge(s_metric, 1)
            pe.wait_ge(s_const, 3)
            pe.wait_ge(s_pool_const, n_pool_const)
            nc.tensor.matmul(ps_misc[:, 0:1], ones[:], small[:, 2:3], start=True, stop=True).then_inc(s_total, 1)
            pe.wait_ge(s_h0, 2)
            for q in range(cdiv(BLOCKS, 4)):
                if q >= 2:
                    pe.wait_ge(s_hid0, q - 1)
                for b in range(4 * q, min(4 * q + 4, BLOCKS)):
                    n = P if b < LAST else ND_LAST
                    last = nc.tensor.transpose((ps_tr, ps_tr2)[q % 2][:, P * (b % 4):P * (b % 4) + n],
                                               h0[0:n, b, :], ident[0:n, 0:n])
                last.then_inc(s_h0tr, 1)
            pe.wait_ge(s_hid0, cdiv(BLOCKS, 4))
            n_w = 3 * GIN + 6
            pe.wait_ge(s_w, 16 * n_w)
            pe.sem_inc(s_mm, TPB)
            for buffer_free in (s_fin, s_tr):
                pe.sem_inc(buffer_free, FREE)
            pe.wait_ge(s_flag, 1)
            fast = pe.value_load(flag[0:1, 0:1], min_val=0, max_val=1)

            def sum_tile(L, slot_rows, slot_sel, n, psum):
                mm = nc.tensor.matmul(ps_sum[psum][:, 0:n], rows[:, slot_rows, :], sel[:, slot_sel, 0:n],
                                      start=True, stop=True)
                if L == 0:
                    mm = nc.tensor.matmul(ps_cnt[psum][:, 0:n], ones[:], sel[:, slot_sel, 0:n],
                                          start=True, stop=True)
                mm.then_inc(s_mm, 1)

            with pe.If(fast != 0):
                for L in range(LAYERS):
                    def tile(j, odd, i, T, tiles, L=L):
                        pe.wait_ge(s_g[i], (j + (L * S_USES(i) + 1)) * 16)
                        pe.wait_ge(s_sel, T + 1)
                        pe.wait_ge(s_add, T + 1)
                        sum_tile(L, i, i, WIN * width(L), (i + odd) % 2)

                    fast_walk(pe, L, T_STAGES, tile)
            with pe.Else():
                for L in range(LAYERS):
                    def tile(t, T, step, L=L):
                        pe.wait_ge(s_g[0], (T + 1) * 16)
                        for c in range(general_steps(L)):
                            pe.wait_ge(s_sel, step + c + 1)
                            pe.wait_ge(s_add, step + c + 2)
                            sum_tile(L, 0, 0, P, 0)

                    general_walk(pe, L, T_STAGES, tile)
            flat = scaled[:].rearrange("p r d -> p (r d)")
            for q in range(cdiv(BLOCKS, 4)):
                pe.wait_ge(s_y, q + 1)
                if q >= 2:
                    pe.wait_ge(s_yout, q - 1)
                for b in range(4 * q, min(4 * q + 4, BLOCKS)):
                    n = P if b < LAST else ND_LAST
                    at = 512 * (q % 2) + P * (b % 4)
                    last = nc.tensor.transpose(ps_sum[q % 2][0:n, D * (b % 4):D * (b % 4) + D],
                                               flat[:, at:at + n], ident[:])
                last.then_inc(s_ytr, 1)


def kernel(x, src, dst, edge_type_8, L0_gnn_W1, L0_gnn_root1, L0_gnn_b1, L0_gnn_W2, L0_gnn_root2, L0_gnn_b2,
           L0_gnn_W3, L0_gnn_root3, L0_gnn_b3, L1_gnn_W1, L1_gnn_b1, L1_gnn_W2, L1_gnn_b2, L1_gnn_gamma,
           L1_gnn_beta):
    import numpy as np
    import concourse.bacc as bacc
    from concourse.bass_utils import run_bass_kernel_spmd

    N, D = x.shape
    edges = src.shape[0]
    tiles, blocks, per_block = plan(N, edges)

    def by_tiles(a, pad):
        padded = np.full(blocks * per_block * P, pad, np.int32)
        padded[:edges] = a
        return np.ascontiguousarray(padded.reshape(-1, P).T)

    t = np.arange(blocks * per_block)
    j, late = t // per_block, t % per_block >= LAG
    lowest = np.where(late, P * j, P * np.maximum(j - 1, 0))
    highest = P * (j + 1 + late) - WIN
    limits = np.stack([lowest, highest]).astype(np.float32)

    arrays = {
        "x": np.asarray(x), "src_t": by_tiles(src, 0), "dst_t": by_tiles(dst, -1),
        "type_t": by_tiles(edge_type_8, 0), "limits": limits,
        "W1": L0_gnn_W1, "W2": L0_gnn_W2, "W3": L0_gnn_W3,
        "root1": L0_gnn_root1, "root2": L0_gnn_root2, "root3": L0_gnn_root3,
        "b1": L0_gnn_b1, "b2": L0_gnn_b2, "b3": L0_gnn_b3,
        "gin_W1": L1_gnn_W1, "gin_b1": L1_gnn_b1, "gin_W2": L1_gnn_W2, "gin_b2": L1_gnn_b2,
        "gamma": L1_gnn_gamma, "beta": L1_gnn_beta,
    }
    arrays = {f"in_{k}": np.ascontiguousarray(v) for k, v in arrays.items()}
    nc = bacc.Bacc("TRN2", target_bir_lowering=False, num_devices=1)
    a = {k[3:]: nc.dram_tensor(k, v.shape, mybir.dt.from_np(v.dtype), kind="ExternalInput").ap()
         for k, v in arrays.items()}
    out = nc.dram_tensor("out", (N, D), F32, kind="ExternalOutput").ap()
    tables = [nc.dram_tensor(f"table{l}", (N, D), F32, kind="Internal").ap() for l in range(LAYERS)]
    gnn_kernel(nc, a["x"], a["src_t"], a["dst_t"], a["type_t"], a["limits"],
               [a["W1"], a["W2"], a["W3"]], [a["root1"], a["root2"], a["root3"]], [a["b1"], a["b2"], a["b3"]],
               a["gin_W1"], a["gin_b1"], a["gin_W2"], a["gin_b2"], a["gamma"], a["beta"], out, tables, edges)
    r = run_bass_kernel_spmd(nc, [arrays], core_ids=[0])
    return r.results[0]["out"]
```
